# Optimizing a Trainium2 kernel written in Bass

```python
import numpy as np
import jax
import jax.numpy as jnp

def _softmax(x, axis=-1):
    return jax.nn.softmax(x, axis=axis)

def _gelu(x):
    return jax.nn.gelu(x, approximate=True)

def _silu(x):
    return jax.nn.silu(x)

def _sigmoid(x):
    return jax.nn.sigmoid(x)

def _layernorm(x, axis=-1, eps=1e-05):
    m = jnp.mean(x, axis=axis, keepdims=True)
    v = jnp.var(x, axis=axis, keepdims=True)
    return (x - m) / jnp.sqrt(v + eps)

def _scatter_add(tgt, idx, src, axis=0):
    return tgt.at[idx].add(src)

def _segment_sum(src, seg, n):
    return jax.ops.segment_sum(src, seg, n)
kernel_name = 'mk_dlrm_tower_d1_rec_r8_40e70d'

def setup_inputs(seed: int=0):
    np.random.seed(seed)
    _w = jnp.asarray

    def _rec_inputs():
        import jax
        import jax.numpy as jnp
        _tk = jax.random.key(seed)
        ids = jnp.stack([jax.random.randint(jax.random.fold_in(_tk, 200 + f), (512,), 0, v, jnp.int32) for f, v in enumerate([1000, 125000, 12500, 1250, 1000, 1000, 1250, 1000, 12500, 1250, 12500, 12500, 1250, 1250, 1250, 1000, 1000, 1000, 12500, 12500, 12500, 1000, 1000, 1000, 1000, 1000])], axis=1)
        tbl_0 = 0.05 * jax.random.normal(jax.random.fold_in(_tk, 500 + 0), (1000, 128), jnp.float32)
        tbl_1 = 0.05 * jax.random.normal(jax.random.fold_in(_tk, 500 + 1), (125000, 128), jnp.float32)
        tbl_2 = 0.05 * jax.random.normal(jax.random.fold_in(_tk, 500 + 2), (12500, 128), jnp.float32)
        tbl_3 = 0.05 * jax.random.normal(jax.random.fold_in(_tk, 500 + 3), (1250, 128), jnp.float32)
        tbl_4 = 0.05 * jax.random.normal(jax.random.fold_in(_tk, 500 + 4), (1000, 128), jnp.float32)
        tbl_5 = 0.05 * jax.random.normal(jax.random.fold_in(_tk, 500 + 5), (1000, 128), jnp.float32)
        tbl_6 = 0.05 * jax.random.normal(jax.random.fold_in(_tk, 500 + 6), (1250, 128), jnp.float32)
        tbl_7 = 0.05 * jax.random.normal(jax.random.fold_in(_tk, 500 + 7), (1000, 128), jnp.float32)
        tbl_8 = 0.05 * jax.random.normal(jax.random.fold_in(_tk, 500 + 8), (12500, 128), jnp.float32)
        tbl_9 = 0.05 * jax.random.normal(jax.random.fold_in(_tk, 500 + 9), (1250, 128), jnp.float32)
        tbl_10 = 0.05 * jax.random.normal(jax.random.fold_in(_tk, 500 + 10), (12500, 128), jnp.float32)
        tbl_11 = 0.05 * jax.random.normal(jax.random.fold_in(_tk, 500 + 11), (12500, 128), jnp.float32)
        tbl_12 = 0.05 * jax.random.normal(jax.random.fold_in(_tk, 500 + 12), (1250, 128), jnp.float32)
        tbl_13 = 0.05 * jax.random.normal(jax.random.fold_in(_tk, 500 + 13), (1250, 128), jnp.float32)
        tbl_14 = 0.05 * jax.random.normal(jax.random.fold_in(_tk, 500 + 14), (1250, 128), jnp.float32)
        tbl_15 = 0.05 * jax.random.normal(jax.random.fold_in(_tk, 500 + 15), (1000, 128), jnp.float32)
        tbl_16 = 0.05 * jax.random.normal(jax.random.fold_in(_tk, 500 + 16), (1000, 128), jnp.float32)
        tbl_17 = 0.05 * jax.random.normal(jax.random.fold_in(_tk, 500 + 17), (1000, 128), jnp.float32)
        tbl_18 = 0.05 * jax.random.normal(jax.random.fold_in(_tk, 500 + 18), (12500, 128), jnp.float32)
        tbl_19 = 0.05 * jax.random.normal(jax.random.fold_in(_tk, 500 + 19), (12500, 128), jnp.float32)
        tbl_20 = 0.05 * jax.random.normal(jax.random.fold_in(_tk, 500 + 20), (12500, 128), jnp.float32)
        tbl_21 = 0.05 * jax.random.normal(jax.random.fold_in(_tk, 500 + 21), (1000, 128), jnp.float32)
        tbl_22 = 0.05 * jax.random.normal(jax.random.fold_in(_tk, 500 + 22), (1000, 128), jnp.float32)
        tbl_23 = 0.05 * jax.random.normal(jax.random.fold_in(_tk, 500 + 23), (1000, 128), jnp.float32)
        tbl_24 = 0.05 * jax.random.normal(jax.random.fold_in(_tk, 500 + 24), (1000, 128), jnp.float32)
        tbl_25 = 0.05 * jax.random.normal(jax.random.fold_in(_tk, 500 + 25), (1000, 128), jnp.float32)
        _rk = jax.random.fold_in(_tk, 7)
        r_bottom_output = -0.000520686 + 1.00062 * jax.random.normal(jax.random.fold_in(_rk, 101), (512, 128), jnp.float32)
        W_top1 = 0.0456912 * jax.random.normal(jax.random.fold_in(_tk, 801), (479, 512), jnp.float32)
        W_top2 = 0.0441942 * jax.random.normal(jax.random.fold_in(_tk, 802), (512, 256), jnp.float32)
        W_top3 = 0.0625 * jax.random.normal(jax.random.fold_in(_tk, 803), (256, 1), jnp.float32)
        b_top1 = jnp.zeros((512,), jnp.float32)
        b_top2 = jnp.zeros((256,), jnp.float32)
        return (r_bottom_output, ids, tbl_0, tbl_1, tbl_2, tbl_3, tbl_4, tbl_5, tbl_6, tbl_7, tbl_8, tbl_9, tbl_10, tbl_11, tbl_12, tbl_13, tbl_14, tbl_15, tbl_16, tbl_17, tbl_18, tbl_19, tbl_20, tbl_21, tbl_22, tbl_23, tbl_24, tbl_25, W_top1, b_top1, W_top2, b_top2, W_top3)
    r_bottom_output, ids, tbl_0, tbl_1, tbl_2, tbl_3, tbl_4, tbl_5, tbl_6, tbl_7, tbl_8, tbl_9, tbl_10, tbl_11, tbl_12, tbl_13, tbl_14, tbl_15, tbl_16, tbl_17, tbl_18, tbl_19, tbl_20, tbl_21, tbl_22, tbl_23, tbl_24, tbl_25, W_top1, b_top1, W_top2, b_top2, W_top3 = _rec_inputs()

    def _L0_rec_setup():
        import jax, jax.numpy as jnp
        import numpy as np
        NUM_FEATURES = 27
        _TRIU_I, _TRIU_J = np.triu_indices(NUM_FEATURES, k=1)
        key = jax.random.key(seed)
        k1, k2 = jax.random.split(key)
        bottom_output = jax.random.normal(k1, (2048, 128), dtype=jnp.float32)
        embeddings = jax.random.normal(k2, (2048, 26, 128), dtype=jnp.float32)
        return {'bottom_output': bottom_output, 'embeddings': embeddings}
    _L0_rec_all = _L0_rec_setup()
    _L0_rec_in = {k: v for k, v in _L0_rec_all.items() if k in ()}
    del _L0_rec_all
    return {'r_bottom_output': r_bottom_output, 'ids': ids, 'tbl_0': tbl_0, 'tbl_1': tbl_1, 'tbl_2': tbl_2, 'tbl_3': tbl_3, 'tbl_4': tbl_4, 'tbl_5': tbl_5, 'tbl_6': tbl_6, 'tbl_7': tbl_7, 'tbl_8': tbl_8, 'tbl_9': tbl_9, 'tbl_10': tbl_10, 'tbl_11': tbl_11, 'tbl_12': tbl_12, 'tbl_13': tbl_13, 'tbl_14': tbl_14, 'tbl_15': tbl_15, 'tbl_16': tbl_16, 'tbl_17': tbl_17, 'tbl_18': tbl_18, 'tbl_19': tbl_19, 'tbl_20': tbl_20, 'tbl_21': tbl_21, 'tbl_22': tbl_22, 'tbl_23': tbl_23, 'tbl_24': tbl_24, 'tbl_25': tbl_25, 'W_top1': W_top1, 'b_top1': b_top1, 'W_top2': W_top2, 'b_top2': b_top2, 'W_top3': W_top3}

def reference(r_bottom_output, ids, tbl_0, tbl_1, tbl_2, tbl_3, tbl_4, tbl_5, tbl_6, tbl_7, tbl_8, tbl_9, tbl_10, tbl_11, tbl_12, tbl_13, tbl_14, tbl_15, tbl_16, tbl_17, tbl_18, tbl_19, tbl_20, tbl_21, tbl_22, tbl_23, tbl_24, tbl_25, W_top1, b_top1, W_top2, b_top2, W_top3):
    import jax
    import jax.numpy as jnp

    def _L0_rec_ref(bottom_output, embeddings):
        import jax, jax.numpy as jnp
        import numpy as np
        NUM_FEATURES = 27
        _TRIU_I, _TRIU_J = np.triu_indices(NUM_FEATURES, k=1)
        all_emb = jnp.concatenate([bottom_output[:, None, :], embeddings], axis=1)
        gram = jnp.einsum('bfd,bgd->bfg', all_emb, all_emb)
        return gram[:, _TRIU_I, _TRIU_J]
    e = jnp.stack([tbl_0[ids[:, 0]], tbl_1[ids[:, 1]], tbl_2[ids[:, 2]], tbl_3[ids[:, 3]], tbl_4[ids[:, 4]], tbl_5[ids[:, 5]], tbl_6[ids[:, 6]], tbl_7[ids[:, 7]], tbl_8[ids[:, 8]], tbl_9[ids[:, 9]], tbl_10[ids[:, 10]], tbl_11[ids[:, 11]], tbl_12[ids[:, 12]], tbl_13[ids[:, 13]], tbl_14[ids[:, 14]], tbl_15[ids[:, 15]], tbl_16[ids[:, 16]], tbl_17[ids[:, 17]], tbl_18[ids[:, 18]], tbl_19[ids[:, 19]], tbl_20[ids[:, 20]], tbl_21[ids[:, 21]], tbl_22[ids[:, 22]], tbl_23[ids[:, 23]], tbl_24[ids[:, 24]], tbl_25[ids[:, 25]]], axis=1)
    z = _L0_rec_ref(r_bottom_output, e)
    z = z.reshape(z.shape[0], -1)
    h = jnp.concatenate([z, r_bottom_output], axis=1)
    h = jnp.maximum(h @ W_top1 + b_top1, 0.0)
    h = jnp.maximum(h @ W_top2 + b_top2, 0.0)
    y = h @ W_top3
    return y

_drawn_inputs = setup_inputs


def setup_inputs(seed=0):
    import zlib

    import numpy as np

    out = dict(_drawn_inputs(seed))
    spreads = {'b_top1': (0.0, 0.1), 'b_top2': (0.0, 0.1)}
    factors = {}
    for name, (base, spread) in spreads.items():
        noise = np.random.default_rng([zlib.crc32(name.encode()), seed]).standard_normal(out[name].shape)
        drawn = base * np.exp(spread * noise) if base else spread * noise
        out[name] = jnp.asarray(drawn.astype(out[name].dtype))
    for name, factor in factors.items():
        out[name] = (out[name] * factor).astype(out[name].dtype)
    return out
```

```python
from contextlib import ExitStack

import concourse.bass as bass
from concourse import mybir

F32 = mybir.dt.float32
F32R = mybir.dt.float32r
I32 = mybir.dt.int32
ALU = mybir.AluOpType
ACT = mybir.ActivationFunctionType

P = 128
BATCH = 512
TILES = BATCH // P
D = 128
TABLE_ROWS = [1000, 125000, 12500, 1250, 1000, 1000, 1250, 1000, 12500, 1250, 12500, 12500, 1250,
              1250, 1250, 1000, 1000, 1000, 12500, 12500, 12500, 1000, 1000, 1000, 1000, 1000]
TABLES = len(TABLE_ROWS)
FEATURES = TABLES + 1
HIDDEN1, HIDDEN2 = 512, 256

ROWS, CHUNKS = 1000, 8
SPREAD = ROWS // CHUNKS
ONE_HOT = [f for f in range(TABLES) if TABLE_ROWS[f] == ROWS][:8]
GATHERED = [f for f in range(TABLES) if f not in ONE_HOT]
POSITIONS = [0] + [f + 1 for f in ONE_HOT] + [f + 1 for f in GATHERED]
FIRST_GATHERED = 1 + len(ONE_HOT)
PER_FILL = 4
GROUPS = [range(i, min(i + PER_FILL, len(GATHERED))) for i in range(0, len(GATHERED), PER_FILL)]

CLASSES = 4
CLASS = P // CLASSES
Z_CHUNKS = -(-FEATURES // CLASSES)
FILL_BANKS = 3
HALF = P // 2


def order_of_work():
    items = [("bottom",), ("one_hot", 0), ("one_hot", 1)]
    items_of_tile = lambda t: [("group", t, k) for k in range(len(GROUPS))]
    waiting = [("one_hot", n) for n in range(2, len(ONE_HOT))]
    for t in range(TILES):
        if t > 0:
            waiting += [("gram", t - 1), ("layer1", t - 1), ("layer2", t - 1), ("layer3", t - 1)]
        for item in items_of_tile(t):
            items.append(item)
            if waiting:
                items.append(waiting.pop(0))
    t = TILES - 1
    return items + waiting + [("gram", t), ("layer1", t), ("layer2", t), ("layer3", t)]


WORK = order_of_work()
FILLS = [w for w in WORK if w[0] in ("bottom", "one_hot", "group")]


def fills_of(engine, before):
    return (before + 1 - engine) // 2


def looked_up(n):
    return FILLS.index(("one_hot", n)) + 1


def build(nc, bottom, ids, ids_by_table, tables, w1_pairs, w1, w2, b2, w3, out):
    with ExitStack() as ctx:
        def sb(name, shape, dt=F32):
            return ctx.enter_context(nc.sbuf_tensor(name, shape, dt))

        def ps(name, shape):
            return ctx.enter_context(nc.psum_tensor(name, shape, F32))

        def sem(name):
            return ctx.enter_context(nc.semaphore(name))

        ids_sb = sb("ids_sb", [P, TILES, TABLES], I32)
        bottom_sb = sb("bottom_sb", [P, TILES, D])
        rows_sb = sb("rows_sb", [P, TILES, len(GATHERED), D])
        feat = sb("feat", [P, BATCH, FEATURES])
        z = sb("z", [P, 2, Z_CHUNKS, P])
        w1p_sb = sb("w1p_sb", [P, Z_CHUNKS, HIDDEN1])
        w1b_sb = sb("w1b_sb", [P, HIDDEN1])
        w2_sb = sb("w2_sb", [P, HIDDEN1 // P, HIDDEN2])
        w3_sb = sb("w3_sb", [P, HIDDEN2 // P])
        b2_sb = sb("b2_sb", [P, HIDDEN2 // P])
        h1 = sb("h1", [P, HIDDEN1 // P, P])
        h2 = sb("h2", [P, HIDDEN2 // P, P])
        y_sb = sb("y_sb", [P, TILES])
        identity = sb("identity", [P, P])
        row_number_i = sb("row_number_i", [P, CHUNKS], I32)
        row_number = sb("row_number", [P, CHUNKS])
        ids_bc = sb("ids_bc", [P, len(ONE_HOT), BATCH], I32)
        table_sb = sb("table_sb", [P, 2, CHUNKS, D])
        table_hi = sb("table_hi", [P, 2, CHUNKS, D], F32R)
        table_lo = sb("table_lo", [P, 2, CHUNKS, D], F32R)
        one_hot = sb("one_hot", [P, 2, CHUNKS, BATCH], F32R)

        fill_ps = [ps(f"fill_ps{i}", [P, BATCH]) for i in range(FILL_BANKS)]
        gram_ps = ps("gram_ps", [P, CLASS, CLASS])
        h1_ps = ps("h1_ps", [P, HIDDEN1 // P, P])
        h2_bank = [ps("h2_ps0", [P, BATCH]), ps("h2_ps1", [P, BATCH])]
        h2_ps = [bank[:, 0:P] for bank in h2_bank]
        y_ps = h2_bank[0][:, P:P + TILES]

        ids_loaded = sem("ids_loaded")
        bottom_loaded = sem("bottom_loaded")
        ids_bc_loaded = sem("ids_bc_loaded")
        table_loaded = [sem(f"table_loaded{i}") for i in range(2)]
        weights_loaded = sem("weights_loaded")
        gathered = [[sem(f"gathered{t}_{k}") for k in range(len(GROUPS))] for t in range(TILES)]
        cleared = sem("cleared")
        identity_ready = sem("identity_ready")
        iota_ready = sem("iota_ready")
        row_number_ready = sem("row_number_ready")
        hi_ready = sem("hi_ready")
        lo_ready = sem("lo_ready")
        one_hot_ready = sem("one_hot_ready")
        z_preset = sem("z_preset")
        filled = sem("filled")
        emptied = [sem("emptied_by_vector"), sem("emptied_by_scalar")]
        gram_done = sem("gram_done")
        z_ready = [sem("z_ready_vector"), sem("z_ready_scalar")]
        layer1_done = sem("layer1_done")
        h1_ready = [sem("h1_ready_vector"), sem("h1_ready_scalar")]
        layer2_done = sem("layer2_done")
        h2_ready = [sem("h2_ready_vector"), sem("h2_ready_scalar")]
        layer3_done = sem("layer3_done")
        y_ready = sem("y_ready")
        stored = sem("stored")

        block = ctx.enter_context(nc.Block())

        @block.sync
        def _(sp):
            sp.dma_start(ids_sb[:], ids.rearrange("(p t) f -> p t f", t=TILES)).then_inc(ids_loaded, 16)

            def load_table(n):
                src = tables[ONE_HOT[n]].rearrange("(p c) d -> p c d", c=CHUNKS)
                most = SPREAD // 16 * 16
                sp.dma_start(table_sb[0:most, n % 2], src[0:most]).then_inc(table_loaded[n % 2], 16)
                sp.dma_start(table_sb[most:SPREAD, n % 2], src[most:SPREAD]).then_inc(table_loaded[n % 2], 16)

            for n, f in enumerate(ONE_HOT):
                sp.dma_start(ids_bc[:, n], ids_by_table[f:f + 1, :].to_broadcast([P, BATCH])).then_inc(ids_bc_loaded, 16)
                if n < 2:
                    load_table(n)
            sp.dma_start(bottom_sb[:], bottom.rearrange("(p t) d -> p t d", t=TILES)).then_inc(bottom_loaded, 16)
            for n in range(2, len(ONE_HOT)):
                sp.wait_ge(lo_ready, n - 1)
                load_table(n)
            sp.dma_start(w1p_sb[:], w1_pairs).then_inc(weights_loaded, 16)
            sp.dma_start(w1b_sb[:], w1[w1.shape[0] - D:, :]).then_inc(weights_loaded, 16)
            sp.dma_start(w2_sb[:], w2.rearrange("(c p) m -> p c m", p=P)).then_inc(weights_loaded, 16)
            sp.dma_start(w3_sb[:], w3.rearrange("(p c) o -> p (c o)", p=P)).then_inc(weights_loaded, 16)
            sp.dma_start(b2_sb[:], b2.rearrange("(p c) -> p c", p=P)).then_inc(weights_loaded, 16)
            sp.wait_ge(y_ready, 1)
            sp.dma_start(out.rearrange("(p t) o -> p (t o)", t=TILES), y_sb[:]).then_inc(stored, 16)
            sp.wait_ge(stored, 16)

        @block.gpsimd
        def _(pool):
            pool.memset(identity[:], 0.0).then_inc(cleared, 1)
            pool.iota(row_number_i[:], pattern=[[1, CHUNKS]], base=0, channel_multiplier=CHUNKS).then_inc(iota_ready, 1)
            pool.wait_ge(cleared, 1)
            pool.affine_select(out=identity[:], in_=identity[:], compare_op=ALU.not_equal, fill=1.0, base=0,
                               pattern=[[-1, P]], channel_multiplier=1).then_inc(identity_ready, 1)
            pool.wait_ge(ids_loaded, 16)
            for t in range(TILES):
                for k, group in enumerate(GROUPS):
                    for i in group:
                        f = GATHERED[i]
                        pool.indirect_dma_start(
                            rows_sb[:, t, i, :], None, tables[f],
                            bass.IndirectOffsetOnAxis(ap=ids_sb[:, t, f:f + 1], axis=0),
                        ).then_inc(gathered[t][k], 16)

        def copy_on(engine):
            return nc.vector.tensor_copy if engine == 0 else nc.scalar.copy

        def empty_fill(eng, engine, n):
            bank = fill_ps[n % FILL_BANKS]
            eng.wait_ge(filled, n + 1)
            item = FILLS[n]
            if item[0] == "bottom":
                src = bank[:].rearrange("d (t p) -> d p t", t=TILES)
                dst = feat[:, :, 0].rearrange("d (p t) -> d p t", t=TILES)
            elif item[0] == "one_hot":
                src, dst = bank[:], feat[:, :, 1 + item[1]]
            else:
                _, t, k = item
                count, first = len(GROUPS[k]), FIRST_GATHERED + GROUPS[k][0]
                src = bank[:, 0:count * P].rearrange("d (i p) -> d p i", i=count)
                dst = feat[:, t::TILES, first:first + count]
            copy_on(engine)(dst, src).then_inc(emptied[engine], 1)

        def empty_gram(eng, engine, t):
            eng.wait_ge(gram_done, t + 1)
            if t >= 2:
                eng.wait_ge(layer1_done, t - 1)
            for j in range(CLASSES):
                if j // 2 != engine:
                    continue
                for c in range(CLASSES):
                    chunks = len(range(c, FEATURES, CLASSES))
                    src = gram_ps[CLASS * j:CLASS * j + FEATURES, :, c:FEATURES:CLASSES]
                    dst = z[CLASS * c:CLASS * c + FEATURES, t % 2, 0:chunks, CLASS * j:CLASS * (j + 1)]
                    last = copy_on(engine)(dst, src.rearrange("f s g -> f g s"))
            last.then_inc(z_ready[engine], 1)

        @block.vector
        def _(dve):
            nc.vector.memset(z[:], 1.0).then_inc(z_preset, 1)
            dve.wait_ge(iota_ready, 1)
            nc.vector.tensor_copy(row_number[:], row_number_i[:]).then_inc(row_number_ready, 1)
            dve.wait_ge(row_number_ready, 1)

            def make_one_hot(n):
                dve.wait_ge(ids_bc_loaded, 16 * len(ONE_HOT))
                if n >= 2:
                    dve.wait_ge(filled, looked_up(n - 2))
                for c in range(CHUNKS):
                    last = nc.vector.tensor_scalar(one_hot[0:SPREAD, n % 2, c], ids_bc[0:SPREAD, n],
                                                   row_number[0:SPREAD, c:c + 1], None, ALU.is_equal)
                last.then_inc(one_hot_ready, 1)
                dve.wait_ge(hi_ready, n + 1)
                nc.vector.tensor_tensor(table_lo[0:SPREAD, n % 2], table_sb[0:SPREAD, n % 2],
                                        table_hi[0:SPREAD, n % 2].bitcast(F32), ALU.subtract).then_inc(lo_ready, 1)

            make_one_hot(0)
            make_one_hot(1)
            for item in WORK:
                if item in FILLS:
                    n = FILLS.index(item)
                    if n % 2 == 0:
                        empty_fill(dve, 0, n)
                    if item[0] == "one_hot" and item[1] + 2 < len(ONE_HOT):
                        make_one_hot(item[1] + 2)
                elif item[0] == "gram":
                    if item[1] == 0:
                        dve.wait_ge(z_preset, 1)
                    empty_gram(dve, 0, item[1])
                elif item[0] == "layer1":
                    dve.wait_ge(layer1_done, item[1] + 1)
                    nc.vector.tensor_scalar_max(h1[0:HALF], h1_ps[0:HALF], 0.0).then_inc(h1_ready[0], 1)
                elif item[0] == "layer2":
                    dve.wait_ge(layer2_done, item[1] + 1)
                    nc.vector.tensor_scalar(h2[:, 0], h2_ps[0], b2_sb[:, 0:1], 0.0, ALU.add, ALU.max).then_inc(h2_ready[0], 1)
            dve.wait_ge(layer3_done, 1)
            nc.vector.tensor_copy(y_sb[:], y_ps).then_inc(y_ready, 1)

        @block.scalar
        def _(act):
            def split_table(n):
                act.wait_ge(table_loaded[n % 2], 32 * (n // 2 + 1))
                if n >= 2:
                    act.wait_ge(filled, looked_up(n - 2))
                nc.scalar.copy(table_hi[0:SPREAD, n % 2], table_sb[0:SPREAD, n % 2]).then_inc(hi_ready, 1)

            split_table(0)
            split_table(1)
            for item in WORK:
                if item in FILLS:
                    n = FILLS.index(item)
                    if n % 2 == 1:
                        empty_fill(act, 1, n)
                    if item[0] == "one_hot" and item[1] + 2 < len(ONE_HOT):
                        split_table(item[1] + 2)
                elif item[0] == "gram":
                    if item[1] == 0:
                        act.wait_ge(z_preset, 1)
                    empty_gram(act, 1, item[1])
                elif item[0] == "layer1":
                    act.wait_ge(layer1_done, item[1] + 1)
                    nc.scalar.activation(h1[HALF:P], h1_ps[HALF:P], ACT.Relu).then_inc(h1_ready[1], 1)
                elif item[0] == "layer2":
                    act.wait_ge(layer2_done, item[1] + 1)
                    nc.scalar.activation(h2[:, 1], h2_ps[1], ACT.Relu, bias=b2_sb[:, 1:2]).then_inc(h2_ready[1], 1)

        @block.tensor
        def _(pe):
            def bank_free(n):
                m = n - FILL_BANKS
                if m >= 0:
                    pe.wait_ge(emptied[m % 2], fills_of(m % 2, m + 1))

            def all_emptied(n):
                for engine in (0, 1):
                    pe.wait_ge(emptied[engine], fills_of(engine, n))

            def fill(n):
                item = FILLS[n]
                bank = fill_ps[n % FILL_BANKS]
                bank_free(n)
                if item[0] == "bottom":
                    pe.wait_ge(identity_ready, 1)
                    pe.wait_ge(bottom_loaded, 16)
                    for t in range(TILES):
                        last = nc.tensor.transpose(bank[:, t * P:(t + 1) * P], bottom_sb[:, t], identity[:])
                    last.then_inc(filled, 1)
                elif item[0] == "group":
                    _, t, k = item
                    pe.wait_ge(gathered[t][k], 16 * len(GROUPS[k]))
                    for at, i in enumerate(GROUPS[k]):
                        last = nc.tensor.transpose(bank[:, at * P:(at + 1) * P], rows_sb[:, t, i], identity[:])
                    last.then_inc(filled, 1)
                else:
                    m = item[1]
                    pe.wait_ge(one_hot_ready, m + 1)
                    pe.wait_ge(lo_ready, m + 1)
                    for c in range(CHUNKS):
                        for part in (table_hi, table_lo):
                            last = nc.tensor.matmul(bank[:], part[0:SPREAD, m % 2, c], one_hot[0:SPREAD, m % 2, c],
                                                    start=(c == 0 and part is table_hi),
                                                    stop=(c == CHUNKS - 1 and part is table_lo))
                    last.then_inc(filled, 1)

            def gram(t, fills_before):
                all_emptied(fills_before)
                if t >= 1:
                    for engine in (0, 1):
                        pe.wait_ge(z_ready[engine], t)
                for s in range(CLASS):
                    for j in range(CLASSES):
                        e = feat[:, TILES * (CLASS * j + s) + t, :]
                        last = nc.tensor.matmul(gram_ps[CLASS * j:CLASS * j + FEATURES, s, 0:FEATURES], e, e,
                                                start=True, stop=True)
                last.then_inc(gram_done, 1)

            def layer1(t):
                if t == 0:
                    pe.wait_ge(weights_loaded, 16 * 5)
                for engine in (0, 1):
                    pe.wait_ge(z_ready[engine], t + 1)
                for nb in range(HIDDEN1 // P):
                    cols = slice(nb * P, (nb + 1) * P)
                    nc.tensor.matmul(h1_ps[:, nb], w1b_sb[:, cols], feat[:, t::TILES, 0], start=True, stop=False)
                    for g in range(Z_CHUNKS):
                        last = nc.tensor.matmul(h1_ps[:, nb], w1p_sb[:, g, cols], z[:, t % 2, g],
                                                start=False, stop=(g == Z_CHUNKS - 1))
                last.then_inc(layer1_done, 1)

            def layer2(t):
                for engine in (0, 1):
                    pe.wait_ge(h1_ready[engine], t + 1)
                for mb in range(HIDDEN2 // P):
                    for nb in range(HIDDEN1 // P):
                        last = nc.tensor.matmul(h2_ps[mb], w2_sb[:, nb, mb::HIDDEN2 // P], h1[:, nb],
                                                start=(nb == 0), stop=(nb == HIDDEN1 // P - 1))
                last.then_inc(layer2_done, 1)

            def layer3(t):
                for engine in (0, 1):
                    pe.wait_ge(h2_ready[engine], t + 1)
                for mb in range(HIDDEN2 // P):
                    last = nc.tensor.matmul(y_ps[:, t:t + 1], h2[:, mb], w3_sb[:, mb:mb + 1],
                                            start=(mb == 0), stop=(mb == HIDDEN2 // P - 1))
                if t == TILES - 1:
                    last.then_inc(layer3_done, 1)

            fills = 0
            for item in WORK:
                if item in FILLS:
                    fill(fills)
                    fills += 1
                elif item[0] == "gram":
                    gram(item[1], fills)
                elif item[0] == "layer1":
                    layer1(item[1])
                elif item[0] == "layer2":
                    layer2(item[1])
                else:
                    layer3(item[1])


def kernel(**inputs):
    import numpy as np
    import concourse.bacc as bacc
    from concourse.bass_utils import run_bass_kernel_spmd

    nc = bacc.Bacc("TRN2", target_bir_lowering=False, num_devices=1)
    arrays = {}

    def give(name, a):
        a = np.ascontiguousarray(a)
        arrays[name] = a
        return nc.dram_tensor(name, a.shape, mybir.dt.from_np(a.dtype), kind="ExternalInput").ap()

    w1 = np.asarray(inputs["W_top1"])
    pair = np.zeros((FEATURES, FEATURES), np.int64)
    pair[np.triu_indices(FEATURES, k=1)] = np.arange(FEATURES * (FEATURES - 1) // 2)
    pairs = np.zeros((P, Z_CHUNKS, HIDDEN1), w1.dtype)
    for j in range(FEATURES):
        for i in range(j):
            lo, hi = sorted((POSITIONS[i], POSITIONS[j]))
            pairs[CLASS * (j % CLASSES) + i, j // CLASSES] = w1[pair[lo, hi]]
    pairs[FEATURES, 0] = np.asarray(inputs["b_top1"])

    ids = np.asarray(inputs["ids"])
    out = nc.dram_tensor("y", (BATCH, 1), F32, kind="ExternalOutput").ap()
    build(nc, give("bottom", inputs["r_bottom_output"]), give("ids", ids), give("ids_by_table", ids.T),
          [give(f"tbl_{f}", inputs[f"tbl_{f}"]) for f in range(TABLES)], give("w1_pairs", pairs), give("w1", w1),
          give("w2", inputs["W_top2"]), give("b2", inputs["b_top2"]), give("w3", inputs["W_top3"]), out)
    return run_bass_kernel_spmd(nc, [arrays], core_ids=[0]).results[0]["y"]
```

```python
from contextlib import ExitStack

import concourse.bass as bass
from concourse import mybir

F32 = mybir.dt.float32
F32R = mybir.dt.float32r
I32 = mybir.dt.int32
ALU = mybir.AluOpType
ACT = mybir.ActivationFunctionType

P = 128
BATCH = 512
TILES = BATCH // P
D = 128
TABLE_ROWS = [1000, 125000, 12500, 1250, 1000, 1000, 1250, 1000, 12500, 1250, 12500, 12500, 1250,
              1250, 1250, 1000, 1000, 1000, 12500, 12500, 12500, 1000, 1000, 1000, 1000, 1000]
TABLES = len(TABLE_ROWS)
FEATURES = TABLES + 1
HIDDEN1, HIDDEN2 = 512, 256

ROWS, CHUNKS = 1000, 8
SPREAD = ROWS // CHUNKS
ONE_HOT = [f for f in range(TABLES) if TABLE_ROWS[f] == ROWS][:7]
GATHERED = [f for f in range(TABLES) if f not in ONE_HOT]
POSITIONS = [0] + [f + 1 for f in ONE_HOT] + [f + 1 for f in GATHERED]
FIRST_GATHERED = 1 + len(ONE_HOT)

PER_FILL = 4
GROUPS = [range(i, min(i + PER_FILL, len(GATHERED))) for i in range(0, len(GATHERED), PER_FILL)]
CLASSES = 4
ROUNDS = 2
CLASS = P // CLASSES
Z_CHUNKS = -(-FEATURES // CLASSES)
FILL_BANKS = 3
W1_CHUNKS = Z_CHUNKS + 1
W1_PIECE = 2
W1_PIECES = W1_CHUNKS // W1_PIECE
BY_SCALAR = (CHUNKS - 1,)
BY_VECTOR = tuple(c for c in range(CHUNKS) if c not in BY_SCALAR)
HALF = P // 2


def order_of_work():
    g = [[("group", t, k) for k in range(len(GROUPS))] for t in range(TILES)]
    look_ups = [("one_hot", n) for n in range(len(ONE_HOT))]
    gram, layer1, turn, layer2, layer3 = ([(kind, t) for t in range(TILES)] for kind in STAGES)

    items = [("bottom",), look_ups[0]]
    early = g[0] + g[1][:2]
    for n, look_up in enumerate(look_ups[1:]):
        items += [look_up] + early[n:n + 1]
    items += early[len(look_ups) - 1:]
    items += [gram[0], g[1][2], layer1[0], g[1][3], turn[0], g[1][4], layer2[0], gram[1]]
    items += [g[2][0], layer3[0], layer1[1], g[2][1], turn[1], g[2][2], g[2][3], g[2][4], layer2[1], gram[2]]
    items += [g[3][0], layer3[1], layer1[2], g[3][1], g[3][2], turn[2], g[3][3], g[3][4], layer2[2], gram[3]]
    return items + [layer3[2], layer1[3], turn[3], layer2[3], layer3[3]]


STAGES = ("gram", "layer1", "turn", "layer2", "layer3")
WORK = order_of_work()
FILLS = [w for w in WORK if w[0] in ("bottom", "one_hot", "group", "turn")]


BEFORE_GRAM = sum(w in FILLS for w in WORK[:WORK.index(("gram", 0))])


def emptied_by(n):
    return 1 if n < BEFORE_GRAM else n % 2


def fills_of(engine, before):
    return sum(emptied_by(n) == engine for n in range(before))


W1_HI_AFTER = [FILLS.index(("one_hot", n)) for n in (1, 2, 3, len(ONE_HOT) - 2)]


def looked_up(n):
    return FILLS.index(("one_hot", n)) + 1


def build(nc, bottom, ids, ids_by_table, tables, w1, w2, b2, w3, out):
    with ExitStack() as ctx:
        def sb(name, shape, dt=F32):
            return ctx.enter_context(nc.sbuf_tensor(name, shape, dt))

        def ps(name, shape):
            return ctx.enter_context(nc.psum_tensor(name, shape, F32))

        def sem(name):
            return ctx.enter_context(nc.semaphore(name))

        ids_sb = sb("ids_sb", [P, TILES, TABLES], I32)
        bottom_sb = sb("bottom_sb", [P, TILES, D])
        rows_sb = sb("rows_sb", [P, 2, len(GATHERED), D])
        feat = sb("feat", [P, BATCH, FEATURES])
        z = sb("z", [P, Z_CHUNKS, CLASSES, ROUNDS, CLASS // ROUNDS])
        z_hi = sb("z_hi", [P, 2, Z_CHUNKS, P], F32R)
        z_lo = sb("z_lo", [P, 2, Z_CHUNKS, P], F32R)
        bottom_hi = sb("bottom_hi", [P, BATCH], F32R)
        bottom_lo = sb("bottom_lo", [P, BATCH], F32R)
        w1_sb = sb("w1_sb", [P, W1_PIECE, HIDDEN1])
        w1_hi = sb("w1_hi", [P, W1_CHUNKS, HIDDEN1], F32R)
        w1_lo = sb("w1_lo", [P, W1_CHUNKS, HIDDEN1], F32R)
        w2_sb = sb("w2_sb", [P, HIDDEN1 // P, HIDDEN2])
        w3_sb = sb("w3_sb", [P, HIDDEN2 // P])
        b2_sb = sb("b2_sb", [P, HIDDEN2 // P])
        h1 = sb("h1", [P, 2, HIDDEN1])
        h1_turned = sb("h1_turned", [P, 2, HIDDEN1 // P, P])
        h2 = sb("h2", [P, HIDDEN2 // P, P])
        y_sb = sb("y_sb", [P, TILES])
        identity = sb("identity", [P, P])
        row_number_i = sb("row_number_i", [P, CHUNKS], I32)
        row_number = sb("row_number", [P, CHUNKS])
        minus_row = sb("minus_row", [P, CHUNKS])
        one = sb("one", [P, 1])
        distance = sb("distance", [P, BATCH], mybir.dt.bfloat16)
        ids_bc = sb("ids_bc", [P, 2, BATCH], I32)
        table_sb = sb("table_sb", [P, 2, CHUNKS, D])
        table_hi = sb("table_hi", [P, 2, CHUNKS, D], F32R)
        table_lo = sb("table_lo", [P, 2, CHUNKS, D], F32R)
        one_hot = sb("one_hot", [P, 2, CHUNKS, BATCH], F32R)

        fill_ps = [ps(f"fill_ps{i}", [P, BATCH]) for i in range(FILL_BANKS)]
        gram_ps = ps("gram_ps", [P, CLASS, CLASS])
        h1_ps = [ps(f"h1_ps{i}", [P, HIDDEN1]) for i in range(2)]
        last_ps = ps("last_ps", [P, BATCH])
        h2_ps = [last_ps[:, mb * P:(mb + 1) * P] for mb in range(HIDDEN2 // P)]
        y_ps = last_ps[:, HIDDEN2:HIDDEN2 + TILES]

        ids_loaded = sem("ids_loaded")
        bottom_loaded = sem("bottom_loaded")
        table_loaded = [sem(f"table_loaded{i}") for i in range(2)]
        weights_loaded = sem("weights_loaded")
        w1_loaded = [sem(f"w1_loaded{i}") for i in range(W1_PIECES)]
        w1_hi_ready = sem("w1_hi_ready")
        w1_lo_ready = sem("w1_lo_ready")
        bottom_hi_ready = sem("bottom_hi_ready")
        bottom_lo_ready = sem("bottom_lo_ready")
        gathered = [[sem(f"gathered{t}_{k}") for k in range(len(GROUPS))] for t in range(TILES)]
        cleared = sem("cleared")
        identity_ready = sem("identity_ready")
        iota_ready = sem("iota_ready")
        one_ready = sem("one_ready")
        row_number_ready = sem("row_number_ready")
        minus_row_ready = sem("minus_row_ready")
        hi_ready = sem("hi_ready")
        lo_ready = sem("lo_ready")
        one_hot_ready = sem("one_hot_ready")
        one_hot_chunk_ready = sem("one_hot_chunk_ready")
        distance_ready = sem("distance_ready")
        z_preset = sem("z_preset")
        filled = sem("filled")
        emptied = [sem("emptied_by_vector"), sem("emptied_by_scalar")]
        gram_done = sem("gram_done")
        z_ready = [sem("z_ready_vector"), sem("z_ready_scalar")]
        z_hi_ready = sem("z_hi_ready")
        z_lo_ready = sem("z_lo_ready")
        layer1_done = sem("layer1_done")
        h1_ready = [sem("h1_ready_vector"), sem("h1_ready_scalar")]
        layer2_done = sem("layer2_done")
        h2_ready = [sem("h2_ready_vector"), sem("h2_ready_scalar")]
        layer3_done = sem("layer3_done")
        y_ready = sem("y_ready")
        stored = sem("stored")

        block = ctx.enter_context(nc.Block())

        w1_pieces = [h1[:], h1_turned[:], w1_sb[:], table_sb[:, len(ONE_HOT) % 2]]
        w1_piece = lambda i: (w1_pieces[i] if i in (0, 2) else w1_pieces[i].rearrange("p a b c -> p a (b c)") if i == 1
                              else w1_pieces[i].rearrange("p (g c) d -> p g (c d)", g=W1_PIECE))

        @block.sync
        def _(sp):
            sp.dma_start(ids_sb[:], ids.rearrange("(p t) f -> p t f", t=TILES)).then_inc(ids_loaded, 16)

            def load_table(n):
                f = ONE_HOT[n]
                sp.dma_start(ids_bc[:, n % 2], ids_by_table[f:f + 1, :].to_broadcast([P, BATCH])).then_inc(table_loaded[n % 2], 16)
                src = tables[f].rearrange("(p c) d -> p c d", c=CHUNKS)
                most = SPREAD // 16 * 16
                sp.dma_start(table_sb[0:most, n % 2], src[0:most]).then_inc(table_loaded[n % 2], 16)
                sp.dma_start(table_sb[most:SPREAD, n % 2], src[most:SPREAD]).then_inc(table_loaded[n % 2], 16)

            def load_w1(i):
                sp.dma_start(w1_piece(i), w1[:, i * W1_PIECE:(i + 1) * W1_PIECE]).then_inc(w1_loaded[i], 16)

            load_table(0)
            sp.dma_start(bottom_sb[:], bottom.rearrange("(p t) d -> p t d", t=TILES)).then_inc(bottom_loaded, 16)
            load_table(1)
            for i in range(W1_PIECES - 1):
                load_w1(i)
            for n in range(2, len(ONE_HOT)):
                sp.wait_ge(lo_ready, n - 1)
                sp.wait_ge(one_hot_chunk_ready, len(BY_SCALAR) * (n - 1))
                load_table(n)
            sp.wait_ge(lo_ready, len(ONE_HOT) - 1)
            load_w1(W1_PIECES - 1)
            sp.dma_start(w2_sb[:], w2.rearrange("(c p) m -> p c m", p=P)).then_inc(weights_loaded, 16)
            sp.dma_start(w3_sb[:], w3.rearrange("(p c) o -> p (c o)", p=P)).then_inc(weights_loaded, 16)
            sp.dma_start(b2_sb[:], b2.rearrange("(p c) -> p c", p=P)).then_inc(weights_loaded, 16)
            sp.wait_ge(y_ready, 1)
            sp.dma_start(out.rearrange("(p t) o -> p (t o)", t=TILES), y_sb[:]).then_inc(stored, 16)
            sp.wait_ge(stored, 16)

        @block.gpsimd
        def _(pool):
            pool.memset(identity[:], 0.0).then_inc(cleared, 1)
            pool.iota(row_number_i[:], pattern=[[1, CHUNKS]], base=0, channel_multiplier=CHUNKS).then_inc(iota_ready, 1)
            pool.wait_ge(cleared, 1)
            pool.affine_select(out=identity[:], in_=identity[:], compare_op=ALU.not_equal, fill=1.0, base=0,
                               pattern=[[-1, P]], channel_multiplier=1).then_inc(identity_ready, 1)
            pool.memset(one[:], 1.0).then_inc(one_ready, 1)
            pool.wait_ge(ids_loaded, 16)
            for t in range(TILES):
                for k, group in enumerate(GROUPS):
                    if t >= 2:
                        pool.wait_ge(filled, FILLS.index(("group", t - 2, k)) + 1)
                    for i in group:
                        f = GATHERED[i]
                        pool.indirect_dma_start(
                            rows_sb[:, t % 2, i, :], None, tables[f],
                            bass.IndirectOffsetOnAxis(ap=ids_sb[:, t, f:f + 1], axis=0),
                        ).then_inc(gathered[t][k], 16)

        def copy_on(engine):
            return nc.vector.tensor_copy if engine == 0 else nc.scalar.copy

        def empty_fill(eng, engine, n):
            bank = fill_ps[n % FILL_BANKS]
            eng.wait_ge(filled, n + 1)
            item = FILLS[n]
            if item[0] == "bottom":
                src = bank[:].rearrange("d (t p) -> d p t", t=TILES)
                dst = feat[:, :, 0].rearrange("d (p t) -> d p t", t=TILES)
                nc.scalar.copy(bottom_hi[:], bank[:]).then_inc(bottom_hi_ready, 1)
            elif item[0] == "one_hot":
                src, dst = bank[:], feat[:, :, 1 + item[1]]
            elif item[0] == "turn":
                src, dst = bank[:], h1_turned[:, item[1] % 2].rearrange("n b p -> n (b p)")
            else:
                _, t, k = item
                count, first = len(GROUPS[k]), FIRST_GATHERED + GROUPS[k][0]
                src = bank[:, 0:count * P].rearrange("d (i p) -> d p i", i=count)
                dst = feat[:, t::TILES, first:first + count]
            copy_on(engine)(dst, src).then_inc(emptied[engine], 1)

        def empty_gram(eng, engine, t, r):
            eng.wait_ge(gram_done, ROUNDS * t + r + 1)
            if t >= 1:
                eng.wait_ge(z_hi_ready, ROUNDS * (t - 1) + r + 1)
                eng.wait_ge(z_lo_ready, ROUNDS * (t - 1) + r + 1)
            samples = slice(r * CLASS // ROUNDS, (r + 1) * CLASS // ROUNDS)
            for j in range(CLASSES):
                if j // 2 != engine:
                    continue
                for c in range(CLASSES):
                    chunks = len(range(c, FEATURES, CLASSES))
                    src = gram_ps[CLASS * j:CLASS * j + FEATURES, samples, c:FEATURES:CLASSES]
                    dst = z[CLASS * c:CLASS * c + FEATURES, 0:chunks, j, r]
                    last = copy_on(engine)(dst, src.rearrange("f s g -> f g s"))
            last.then_inc(z_ready[engine], 1)

        def round_of(tensor, r):
            return tensor.rearrange("k c (j r s) -> k c j r s", j=CLASSES, r=ROUNDS)[:, :, :, r]

        @block.vector
        def _(dve):
            nc.vector.memset(z[:], 1.0).then_inc(z_preset, 1)
            dve.wait_ge(iota_ready, 1)
            nc.vector.tensor_copy(row_number[:], row_number_i[:]).then_inc(row_number_ready, 1)
            dve.wait_ge(row_number_ready, 1)
            def make_one_hot(n):
                dve.wait_ge(table_loaded[n % 2], 48 * (n // 2 + 1))
                if n >= 2:
                    dve.wait_ge(filled, looked_up(n - 2))
                for c in BY_VECTOR:
                    nc.vector.tensor_scalar(one_hot[0:SPREAD, n % 2, c], ids_bc[0:SPREAD, n % 2],
                                            row_number[0:SPREAD, c:c + 1], None, ALU.is_equal).then_inc(one_hot_ready, 1)
                dve.wait_ge(hi_ready, n + 1)
                nc.vector.tensor_tensor(table_lo[0:SPREAD, n % 2], table_sb[0:SPREAD, n % 2],
                                        table_hi[0:SPREAD, n % 2].bitcast(F32), ALU.subtract).then_inc(lo_ready, 1)

            def split_w1(i):
                dve.wait_ge(w1_hi_ready, i + 1)
                nc.vector.tensor_tensor(w1_lo[:, i * W1_PIECE:(i + 1) * W1_PIECE], w1_piece(i),
                                        w1_hi[:, i * W1_PIECE:(i + 1) * W1_PIECE].bitcast(F32),
                                        ALU.subtract).then_inc(w1_lo_ready, 1)

            make_one_hot(0)
            make_one_hot(1)
            for item in WORK:
                if item in FILLS:
                    n = FILLS.index(item)
                    if emptied_by(n) == 0:
                        empty_fill(dve, 0, n)
                    if item[0] == "bottom":
                        dve.wait_ge(emptied[1], 1)
                        nc.vector.tensor_tensor(bottom_lo[:].rearrange("d (t p) -> d t p", t=TILES),
                                                feat[:, :, 0].rearrange("d (p t) -> d t p", t=TILES),
                                                bottom_hi[:].bitcast(F32).rearrange("d (t p) -> d t p", t=TILES),
                                                ALU.subtract).then_inc(bottom_lo_ready, 1)
                    if item[0] == "one_hot" and item[1] + 2 < len(ONE_HOT):
                        make_one_hot(item[1] + 2)
                    if item == ("one_hot", len(ONE_HOT) - 3):
                        for i in range(W1_PIECES):
                            split_w1(i)
                elif item[0] == "gram":
                    t = item[1]
                    if t == 0:
                        dve.wait_ge(z_preset, 1)
                    for r in range(ROUNDS):
                        empty_gram(dve, 0, t, r)
                    for r in range(ROUNDS):
                        dve.wait_ge(z_hi_ready, ROUNDS * t + r + 1)
                        nc.vector.tensor_tensor(round_of(z_lo[:, t % 2], r), z[:, :, :, r], round_of(z_hi[:, t % 2].bitcast(F32), r),
                                                ALU.subtract).then_inc(z_lo_ready, 1)
                elif item[0] == "layer1":
                    t = item[1]
                    dve.wait_ge(layer1_done, t + 1)
                    nc.vector.tensor_scalar_max(h1[0:HALF, t % 2], h1_ps[t % 2][0:HALF], 0.0).then_inc(h1_ready[0], 1)
                elif item[0] == "layer2":
                    dve.wait_ge(layer2_done, item[1] + 1)
                    for mb in range(HIDDEN2 // P):
                        last = nc.vector.tensor_scalar(h2[0:HALF, mb], h2_ps[mb][0:HALF], b2_sb[0:HALF, mb:mb + 1], 0.0,
                                                       ALU.add, ALU.max)
                    last.then_inc(h2_ready[0], 1)
            dve.wait_ge(layer3_done, 1)
            nc.vector.tensor_copy(y_sb[:], y_ps).then_inc(y_ready, 1)

        @block.scalar
        def _(act):
            def split_table(n):
                act.wait_ge(table_loaded[n % 2], 48 * (n // 2 + 1))
                if n >= 2:
                    act.wait_ge(filled, looked_up(n - 2))
                nc.scalar.copy(table_hi[0:SPREAD, n % 2], table_sb[0:SPREAD, n % 2]).then_inc(hi_ready, 1)
                for at, c in enumerate(BY_SCALAR):
                    done = n * len(BY_SCALAR) + at
                    if done:
                        act.wait_ge(one_hot_chunk_ready, done)
                    nc.scalar.activation(distance[0:SPREAD], ids_bc[0:SPREAD, n % 2], ACT.Abs,
                                         bias=minus_row[0:SPREAD, c:c + 1]).then_inc(distance_ready, 1)
                    act.wait_ge(distance_ready, done + 1)
                    nc.scalar.activation(one_hot[0:SPREAD, n % 2, c], distance[0:SPREAD], ACT.Relu,
                                         bias=one[0:SPREAD], scale=-1.0).then_inc(one_hot_chunk_ready, 1)

            def split_w1(i):
                act.wait_ge(w1_loaded[i], 16)
                nc.scalar.copy(w1_hi[:, i * W1_PIECE:(i + 1) * W1_PIECE], w1_piece(i)).then_inc(w1_hi_ready, 1)

            act.wait_ge(row_number_ready, 1)
            nc.scalar.mul(minus_row[:], row_number[:], -1.0).then_inc(minus_row_ready, 1)
            act.wait_ge(minus_row_ready, 1)
            act.wait_ge(one_ready, 1)
            split_table(0)
            split_table(1)
            for item in WORK:
                if item in FILLS:
                    n = FILLS.index(item)
                    if emptied_by(n) == 1:
                        empty_fill(act, 1, n)
                    if item[0] == "one_hot" and item[1] + 2 < len(ONE_HOT):
                        split_table(item[1] + 2)
                    if n in W1_HI_AFTER:
                        split_w1(W1_HI_AFTER.index(n))
                elif item[0] == "gram":
                    t = item[1]
                    if t == 0:
                        act.wait_ge(z_preset, 1)
                    for r in range(ROUNDS):
                        empty_gram(act, 1, t, r)
                        act.wait_ge(z_ready[0], ROUNDS * t + r + 1)
                        act.wait_ge(z_ready[1], ROUNDS * t + r + 1)
                        if t >= 2:
                            act.wait_ge(layer1_done, t - 1)
                        nc.scalar.copy(round_of(z_hi[:, t % 2], r), z[:, :, :, r]).then_inc(z_hi_ready, 1)
                elif item[0] == "layer1":
                    t = item[1]
                    act.wait_ge(layer1_done, t + 1)
                    nc.scalar.activation(h1[HALF:P, t % 2], h1_ps[t % 2][HALF:P], ACT.Relu).then_inc(h1_ready[1], 1)
                elif item[0] == "layer2":
                    act.wait_ge(layer2_done, item[1] + 1)
                    for mb in range(HIDDEN2 // P):
                        last = nc.scalar.activation(h2[HALF:P, mb], h2_ps[mb][HALF:P], ACT.Relu, bias=b2_sb[HALF:P, mb:mb + 1])
                    last.then_inc(h2_ready[1], 1)

        @block.tensor
        def _(pe):
            def bank_free(n):
                m = n - FILL_BANKS
                if m >= 0:
                    pe.wait_ge(emptied[emptied_by(m)], fills_of(emptied_by(m), m + 1))

            def all_emptied(n):
                for engine in (0, 1):
                    pe.wait_ge(emptied[engine], fills_of(engine, n))

            def fill(n):
                item = FILLS[n]
                bank = fill_ps[n % FILL_BANKS]
                bank_free(n)
                if item[0] == "bottom":
                    pe.wait_ge(identity_ready, 1)
                    pe.wait_ge(bottom_loaded, 16)
                    for t in range(TILES):
                        last = nc.tensor.transpose(bank[:, t * P:(t + 1) * P], bottom_sb[:, t], identity[:])
                    last.then_inc(filled, 1)
                elif item[0] == "group":
                    _, t, k = item
                    pe.wait_ge(gathered[t][k], 16 * len(GROUPS[k]))
                    for at, i in enumerate(GROUPS[k]):
                        last = nc.tensor.transpose(bank[:, at * P:(at + 1) * P], rows_sb[:, t % 2, i], identity[:])
                    last.then_inc(filled, 1)
                elif item[0] == "turn":
                    for engine in (0, 1):
                        pe.wait_ge(h1_ready[engine], item[1] + 1)
                    for nb in range(HIDDEN1 // P):
                        last = nc.tensor.transpose(bank[:, nb * P:(nb + 1) * P], h1[:, item[1] % 2, nb * P:(nb + 1) * P], identity[:])
                    last.then_inc(filled, 1)
                else:
                    m = item[1]
                    pe.wait_ge(hi_ready, m + 1)
                    for c in range(CHUNKS):
                        if c in BY_SCALAR:
                            pe.wait_ge(one_hot_chunk_ready, len(BY_SCALAR) * m + BY_SCALAR.index(c) + 1)
                        else:
                            pe.wait_ge(one_hot_ready, len(BY_VECTOR) * m + BY_VECTOR.index(c) + 1)
                        nc.tensor.matmul(bank[:], table_hi[0:SPREAD, m % 2, c], one_hot[0:SPREAD, m % 2, c],
                                         start=(c == 0), stop=False)
                    pe.wait_ge(lo_ready, m + 1)
                    for c in range(CHUNKS):
                        last = nc.tensor.matmul(bank[:], table_lo[0:SPREAD, m % 2, c], one_hot[0:SPREAD, m % 2, c],
                                                start=False, stop=(c == CHUNKS - 1))
                    last.then_inc(filled, 1)

            def gram(t, fills_before):
                all_emptied(fills_before)
                for r in range(ROUNDS):
                    if t >= 1:
                        for engine in (0, 1):
                            pe.wait_ge(z_ready[engine], ROUNDS * (t - 1) + r + 1)
                    for s in range(r * CLASS // ROUNDS, (r + 1) * CLASS // ROUNDS):
                        for j in range(CLASSES):
                            e = feat[:, TILES * (CLASS * j + s) + t, :]
                            last = nc.tensor.matmul(gram_ps[CLASS * j:CLASS * j + FEATURES, s, 0:FEATURES], e, e,
                                                    start=True, stop=True)
                    last.then_inc(gram_done, 1)

            def layer1(t):
                into = h1_ps[t % 2]
                if t == 0:
                    pe.wait_ge(bottom_lo_ready, 1)
                    pe.wait_ge(w1_lo_ready, W1_PIECES)
                if t >= 2:
                    for engine in (0, 1):
                        pe.wait_ge(h1_ready[engine], t - 1)
                tile = slice(t * P, (t + 1) * P)
                for x, w in ((bottom_hi, w1_hi), (bottom_hi, w1_lo), (bottom_lo, w1_hi)):
                    nc.tensor.matmul(into[:], x[:, tile], w[:, Z_CHUNKS],
                                     start=(x is bottom_hi and w is w1_hi), stop=False)
                pe.wait_ge(z_hi_ready, ROUNDS * (t + 1))
                for g in range(Z_CHUNKS):
                    nc.tensor.matmul(into[:], z_hi[:, t % 2, g], w1_hi[:, g], start=False, stop=False)
                    nc.tensor.matmul(into[:], z_hi[:, t % 2, g], w1_lo[:, g], start=False, stop=False)
                pe.wait_ge(z_lo_ready, ROUNDS * (t + 1))
                for g in range(Z_CHUNKS):
                    last = nc.tensor.matmul(into[:], z_lo[:, t % 2, g], w1_hi[:, g], start=False, stop=(g == Z_CHUNKS - 1))
                last.then_inc(layer1_done, 1)

            def layer2(t, fills_before):
                if t == 0:
                    pe.wait_ge(weights_loaded, 16 * 3)
                all_emptied(fills_before)
                for mb in range(HIDDEN2 // P):
                    for nb in range(HIDDEN1 // P):
                        last = nc.tensor.matmul(h2_ps[mb], w2_sb[:, nb, mb::HIDDEN2 // P], h1_turned[:, t % 2, nb],
                                                start=(nb == 0), stop=(nb == HIDDEN1 // P - 1))
                last.then_inc(layer2_done, 1)

            def layer3(t):
                for engine in (0, 1):
                    pe.wait_ge(h2_ready[engine], t + 1)
                for mb in range(HIDDEN2 // P):
                    last = nc.tensor.matmul(y_ps[:, t:t + 1], h2[:, mb], w3_sb[:, mb:mb + 1],
                                            start=(mb == 0), stop=(mb == HIDDEN2 // P - 1))
                if t == TILES - 1:
                    last.then_inc(layer3_done, 1)

            fills = 0
            for item in WORK:
                if item in FILLS:
                    fill(fills)
                    fills += 1
                elif item[0] == "gram":
                    gram(item[1], fills)
                elif item[0] == "layer1":
                    layer1(item[1])
                elif item[0] == "layer2":
                    layer2(item[1], fills)
                else:
                    layer3(item[1])


def kernel(**inputs):
    import numpy as np
    import concourse.bacc as bacc
    from concourse.bass_utils import run_bass_kernel_spmd

    nc = bacc.Bacc("TRN2", target_bir_lowering=False, num_devices=1)
    arrays = {}

    def give(name, a):
        a = np.ascontiguousarray(a)
        arrays[name] = a
        return nc.dram_tensor(name, a.shape, mybir.dt.from_np(a.dtype), kind="ExternalInput").ap()

    w1 = np.asarray(inputs["W_top1"])
    pair = np.zeros((FEATURES, FEATURES), np.int64)
    pair[np.triu_indices(FEATURES, k=1)] = np.arange(FEATURES * (FEATURES - 1) // 2)
    pairs = np.zeros((P, W1_CHUNKS, HIDDEN1), w1.dtype)
    for j in range(FEATURES):
        for i in range(j):
            lo, hi = sorted((POSITIONS[i], POSITIONS[j]))
            pairs[CLASS * (j % CLASSES) + i, j // CLASSES] = w1[pair[lo, hi]]
    pairs[FEATURES, 0] = np.asarray(inputs["b_top1"])
    pairs[:, Z_CHUNKS] = w1[w1.shape[0] - D:]

    ids = np.asarray(inputs["ids"])
    out = nc.dram_tensor("y", (BATCH, 1), F32, kind="ExternalOutput").ap()
    build(nc, give("bottom", inputs["r_bottom_output"]), give("ids", ids), give("ids_by_table", ids.T),
          [give(f"tbl_{f}", inputs[f"tbl_{f}"]) for f in range(TABLES)], give("w1", pairs),
          give("w2", inputs["W_top2"]), give("b2", inputs["b_top2"]), give("w3", inputs["W_top3"]), out)
    return run_bass_kernel_spmd(nc, [arrays], core_ids=[0]).results[0]["y"]
```

```python
from contextlib import ExitStack

import concourse.bass as bass
from concourse import mybir

F32 = mybir.dt.float32
F32R = mybir.dt.float32r
I32 = mybir.dt.int32
ALU = mybir.AluOpType
ACT = mybir.ActivationFunctionType

P = 128
BATCH = 512
TILES = BATCH // P
LAST = TILES - 1
D = 128
TABLE_ROWS = [1000, 125000, 12500, 1250, 1000, 1000, 1250, 1000, 12500, 1250, 12500, 12500, 1250,
              1250, 1250, 1000, 1000, 1000, 12500, 12500, 12500, 1000, 1000, 1000, 1000, 1000]
TABLES = len(TABLE_ROWS)
FEATURES = TABLES + 1
HIDDEN1, HIDDEN2 = 512, 256

ROWS, CHUNKS = 1000, 8
SPREAD = ROWS // CHUNKS
ONE_HOT = [f for f in range(TABLES) if TABLE_ROWS[f] == ROWS][:8]
GATHERED = sorted((f for f in range(TABLES) if f not in ONE_HOT), key=lambda f: TABLE_ROWS[f] == ROWS)
POSITIONS = [0] + [f + 1 for f in ONE_HOT] + [f + 1 for f in GATHERED]
FIRST_GATHERED = 1 + len(ONE_HOT)
LATE_TABLE = GATHERED[-1]
LATE_FROM = 2
LATE_SAMPLES = BATCH // TILES * (TILES - LATE_FROM)
LOOKED_UP = ONE_HOT + [LATE_TABLE]
LATE = len(ONE_HOT)

PER_FILL = 4
GROUPS = [range(i, min(i + PER_FILL, len(GATHERED))) for i in range(0, len(GATHERED), PER_FILL)]
FILL_BANKS = 4

CLASSES = 4
CLASS = P // CLASSES
ROUNDS = 2
Z_CHUNKS = -(-FEATURES // CLASSES)

W1_CHUNKS = Z_CHUNKS + 1
W1_PIECE = 2
W1_PIECES = W1_CHUNKS // W1_PIECE
HALF = P // 2

BY_SCALAR = (CHUNKS - 1,)
BY_VECTOR = tuple(c for c in range(CHUNKS) if c not in BY_SCALAR)
LOW_PART_AT = 4
RAW_BUFFERS = 5
IDS_BUFFERS = 3
WARM_UP = 24


def group(t, k):
    return [i for i in GROUPS[k] if t < LATE_FROM or GATHERED[i] != LATE_TABLE]


def order_of_work():
    g = [[("group", t, k) for k in range(len(GROUPS))] for t in range(TILES)]
    look_ups = [("one_hot", n) for n in range(len(ONE_HOT))]
    gram, layer1, turn, layer2 = ([(kind, t) for t in range(TILES)] for kind in STAGES)
    last_turns = [("turn", LAST, half) for half in range(2)]

    late = ("one_hot", LATE)
    items = [("bottom",), look_ups[0]]
    between = g[0] + g[1][:2]
    for n, look_up in enumerate(look_ups[1:]):
        items += [look_up] + between[n:n + 1]
    items += [gram[0]] + g[1][2:] + [layer1[0], late, turn[0]]
    items += [gram[1], layer2[0], layer1[1]] + g[2] + [turn[1]]
    items += [gram[2], layer2[1], layer1[2]] + g[3] + [turn[2]]
    items += [gram[3], layer2[2], layer1[3]]
    items += [last_turns[0], ("bias", LAST), last_turns[1], layer2[3]]
    return [w for item in items for w in ([("bias", item[1]), item] if item in layer2[:LAST] else [item])]


def order_of_loads():
    return ([("table", n) for n in range(len(ONE_HOT))] + [("w1", i) for i in range(W1_PIECES)] +
            [("table", LATE)])


STAGES = ("gram", "layer1", "turn", "layer2")
WORK = order_of_work()
LOADS = order_of_loads()
FILLS = [w for w in WORK if w[0] in ("bottom", "one_hot", "group", "turn")]
TURNS = [w for w in WORK if w[0] == "turn"]
BEFORE_GRAM = sum(w in FILLS for w in WORK[:WORK.index(("gram", 0))])
W1_AFTER = [FILLS.index(("one_hot", len(ONE_HOT) - n)) for n in (3, 2, 2, 1)]


def emptied_by(n):
    if FILLS[n][0] == "turn":
        return 0
    return 1 if n < BEFORE_GRAM else n % 2


def needed_by(t):
    needed = [FILLS.index(w) for w in FILLS if w[:2] == ("group", t) or w[0] == "bottom" or
              w[0] == "one_hot" and (w[1] < LATE or t >= LATE_FROM)]
    return max(needed) + 1


def fills_of(engine, before):
    return sum(emptied_by(n) == engine for n in range(before))


def looked_up(n):
    return FILLS.index(("one_hot", n)) + 1


def build(nc, bottom, ids, ids_by_table, tables, w1, w2, b2, w3, out):
    with ExitStack() as ctx:
        def sb(name, shape, dt=F32):
            return ctx.enter_context(nc.sbuf_tensor(name, shape, dt))

        def ps(name, shape):
            return ctx.enter_context(nc.psum_tensor(name, shape, F32))

        def sem(name):
            return ctx.enter_context(nc.semaphore(name))

        ids_sb = sb("ids_sb", [P, TILES, TABLES], I32)
        bottom_sb = sb("bottom_sb", [P, TILES, D])
        rows_sb = sb("rows_sb", [P, 2, len(GATHERED), D])
        feat = sb("feat", [P, BATCH, FEATURES])
        z = sb("z", [P, Z_CHUNKS, CLASSES, ROUNDS, CLASS // ROUNDS])
        z_hi = sb("z_hi", [P, 2, Z_CHUNKS, P], F32R)
        z_lo = sb("z_lo", [P, 2, Z_CHUNKS, P], F32R)
        bottom_hi = sb("bottom_hi", [P, BATCH], F32R)
        bottom_lo = sb("bottom_lo", [P, BATCH], F32R)
        w1_hi = sb("w1_hi", [P, W1_CHUNKS, HIDDEN1], F32R)
        w1_lo = sb("w1_lo", [P, W1_CHUNKS, HIDDEN1], F32R)
        w2_sb = sb("w2_sb", [P, HIDDEN1 // P, HIDDEN2])
        h1 = sb("h1", [P, 2, HIDDEN1])
        y_sb = sb("y_sb", [P, TILES])
        identity = sb("identity", [P, P])
        row_number_i = sb("row_number_i", [P, CHUNKS], I32)
        row_number = sb("row_number", [P, CHUNKS])
        minus_row = sb("minus_row", [P, CHUNKS])
        one = sb("one", [P, 1])
        distance = sb("distance", [P, BATCH], mybir.dt.bfloat16)
        ids_spread_sb = sb("ids_spread_sb", [P, IDS_BUFFERS, BATCH], I32)
        raw_sb = sb("raw_sb", [P, RAW_BUFFERS - 1, CHUNKS, D])
        table_hi = sb("table_hi", [P, 2, CHUNKS, D], F32R)
        table_lo = sb("table_lo", [P, 2, CHUNKS, D], F32R)
        one_hot = sb("one_hot", [P, 2, CHUNKS, BATCH], F32R)

        fill_ps = [ps(f"fill_ps{i}", [P, BATCH]) for i in range(FILL_BANKS)]
        gram_ps = ps("gram_ps", [P, CLASS, CLASS])
        h1_ps = ps("h1_ps", [P, HIDDEN1])
        h1_ps_last = gram_ps[:, 0:HIDDEN1 // CLASS].rearrange("p s g -> p (s g)")
        h2_ps = ps("h2_ps", [P, BATCH])[:, 0:HIDDEN2]

        freed = one_hot[:, 1]
        w2_hi, w2_lo = (freed[:, 2 * i:2 * i + 2].rearrange("p c (h n) -> p (c h) n", n=HIDDEN2) for i in (0, 1))
        turned_hi, turned_lo = (freed[:, 2 * i:2 * i + 2].rearrange("p t (b s) -> p t b s", s=P) for i in (2, 3))
        row = table_hi[0:1, 1].rearrange("p c d -> p (c d)")
        b2_hi, b2_lo, ones = row[:, 0:HIDDEN2], row[:, HIDDEN2:2 * HIDDEN2], row[:, 2 * HIDDEN2:2 * HIDDEN2 + P]
        spare = raw_sb[:, RAW_BUFFERS - 2].rearrange("p c d -> p (c d)")
        w3_spread, h2 = spare[:, 0:HIDDEN2], spare[:, HIDDEN2:2 * HIDDEN2]
        b2_row = spare[0:1, 2 * HIDDEN2:3 * HIDDEN2]

        ids_loaded = sem("ids_loaded")
        bottom_loaded = sem("bottom_loaded")
        ids_spread = [sem(f"ids_spread{n}") for n in range(len(LOOKED_UP))]
        table_loaded = [sem(f"table_loaded{n}") for n in range(len(LOOKED_UP))]
        weights_loaded = sem("weights_loaded")
        w1_loaded = [sem(f"w1_loaded{i}") for i in range(W1_PIECES)]
        w1_hi_ready = sem("w1_hi_ready")
        w1_lo_ready = sem("w1_lo_ready")
        bottom_hi_ready = sem("bottom_hi_ready")
        bottom_lo_ready = sem("bottom_lo_ready")
        gathered = [[sem(f"gathered{t}_{k}") for k in range(len(GROUPS))] for t in range(TILES)]
        cleared = sem("cleared")
        identity_ready = sem("identity_ready")
        iota_ready = sem("iota_ready")
        one_ready = sem("one_ready")
        row_number_ready = sem("row_number_ready")
        minus_row_ready = sem("minus_row_ready")
        table_hi_ready = sem("table_hi_ready")
        table_lo_ready = sem("table_lo_ready")
        one_hot_by_vector_ready = sem("one_hot_by_vector_ready")
        one_hot_by_scalar_ready = sem("one_hot_by_scalar_ready")
        distance_ready = sem("distance_ready")
        z_preset = sem("z_preset")
        filled = sem("filled")
        emptied = [sem("emptied_by_vector"), sem("emptied_by_scalar")]
        gram_done = sem("gram_done")
        z_ready = [sem("z_ready_vector"), sem("z_ready_scalar")]
        z_hi_ready = sem("z_hi_ready")
        z_lo_ready = sem("z_lo_ready")
        layer1_done = sem("layer1_done")
        h1_ready = [sem("h1_ready_vector"), sem("h1_ready_scalar")]
        layer2_done = sem("layer2_done")
        turned_hi_ready = sem("turned_hi_ready")
        w2_hi_ready = sem("w2_hi_ready")
        w2_lo_ready = sem("w2_lo_ready")
        b2_hi_ready = sem("b2_hi_ready")
        b2_lo_ready = sem("b2_lo_ready")
        ones_ready = sem("ones_ready")
        y_ready = sem("y_ready")
        stored = sem("stored")

        block = ctx.enter_context(nc.Block())

        def raw(kind, i):
            m = LOADS.index((kind, i)) % RAW_BUFFERS
            flat = (h1[:].rearrange("p t n -> p (t n)") if m == RAW_BUFFERS - 1 else
                    raw_sb[:, m].rearrange("p c d -> p (c d)"))
            return flat.rearrange("p (c d) -> p c d", c=CHUNKS if kind == "table" else W1_PIECE)

        def ids_bc(n):
            return ids_spread_sb[:, n % IDS_BUFFERS]

        def late(tensor):
            return tensor.rearrange("p (b t) -> p b t", t=TILES)[:, :, LATE_FROM:]

        def samples_looked_up(n):
            return LATE_SAMPLES if n == LATE else BATCH

        def ids_looked_up(n):
            return late(ids_bc(n)[0:SPREAD]) if n == LATE else ids_bc(n)[0:SPREAD]

        def one_hot_chunk(n, c):
            return one_hot[0:SPREAD, n % 2, c, 0:samples_looked_up(n)]

        def like_ids(tensor, n):
            return tensor.rearrange("p (b t) -> p b t", t=TILES - LATE_FROM) if n == LATE else tensor

        @block.sync
        def _(sp):
            sp.dma_start(ids_sb[:], ids.rearrange("(p t) f -> p t f", t=TILES)).then_inc(ids_loaded, 16)

            def load_ids(n):
                f = LOOKED_UP[n]
                if n >= IDS_BUFFERS:
                    sp.wait_ge(one_hot_by_vector_ready, len(BY_VECTOR) * (n - IDS_BUFFERS + 1))
                    sp.wait_ge(one_hot_by_scalar_ready, len(BY_SCALAR) * (n - IDS_BUFFERS + 1))
                sp.dma_start(ids_bc(n), ids_by_table[f:f + 1, :].to_broadcast([P, BATCH])).then_inc(ids_spread[n], 16)

            def load(m):
                if m >= RAW_BUFFERS:
                    kind, i = LOADS[m - RAW_BUFFERS]
                    sp.wait_ge(table_lo_ready if kind == "table" else w1_lo_ready, i + 1)
                kind, i = LOADS[m]
                if kind == "table":
                    src = tables[LOOKED_UP[i]].rearrange("(p c) d -> p c d", c=CHUNKS)
                    most = SPREAD // 16 * 16
                    sp.dma_start(raw(kind, i)[0:most], src[0:most]).then_inc(table_loaded[i], 16)
                    sp.dma_start(raw(kind, i)[most:SPREAD], src[most:SPREAD]).then_inc(table_loaded[i], 16)
                else:
                    sp.dma_start(raw(kind, i), w1[:, i * W1_PIECE:(i + 1) * W1_PIECE]).then_inc(w1_loaded[i], 16)

            load_ids(0)
            load(0)
            sp.dma_start(bottom_sb[:], bottom.rearrange("(p t) d -> p t d", t=TILES)).then_inc(bottom_loaded, 16)
            for m in range(1, RAW_BUFFERS):
                if m < IDS_BUFFERS:
                    load_ids(m)
                load(m)
            for n in range(max(len(LOADS) - RAW_BUFFERS, len(LOOKED_UP) - IDS_BUFFERS)):
                if n + IDS_BUFFERS < len(LOOKED_UP):
                    load_ids(n + IDS_BUFFERS)
                if n + RAW_BUFFERS < len(LOADS):
                    load(n + RAW_BUFFERS)
            sp.dma_start(w2_sb[:], w2.rearrange("(c p) m -> p c m", p=P)).then_inc(weights_loaded, 16)
            kind, i = [what for m, what in enumerate(LOADS) if m % RAW_BUFFERS == RAW_BUFFERS - 2][-1]
            sp.wait_ge(table_lo_ready if kind == "table" else w1_lo_ready, i + 1)
            sp.dma_start(w3_spread, w3.rearrange("n o -> o n").to_broadcast([P, HIDDEN2])).then_inc(weights_loaded, 16)
            sp.dma_start(b2_row, b2.rearrange("(o n) -> o n", o=1)).then_inc(weights_loaded, 16)
            sp.wait_ge(y_ready, TILES)
            sp.dma_start(out.rearrange("(p t) o -> p (t o)", t=TILES), y_sb[:]).then_inc(stored, 16)
            sp.wait_ge(stored, 16)

        @block.gpsimd
        def _(pool):
            pool.memset(identity[:], 0.0).then_inc(cleared, 1)
            pool.iota(row_number_i[:], pattern=[[1, CHUNKS]], base=0, channel_multiplier=CHUNKS).then_inc(iota_ready, 1)
            pool.wait_ge(cleared, 1)
            pool.affine_select(out=identity[:], in_=identity[:], compare_op=ALU.not_equal, fill=1.0, base=0,
                               pattern=[[-1, P]], channel_multiplier=1).then_inc(identity_ready, 1)
            pool.memset(one[:], 1.0).then_inc(one_ready, 1)
            pool.wait_ge(ids_loaded, 16)
            for t in range(TILES):
                for k in range(len(GROUPS)):
                    if t >= 2:
                        pool.wait_ge(filled, FILLS.index(("group", t - 2, k)) + 1)
                    for i in group(t, k):
                        f = GATHERED[i]
                        pool.indirect_dma_start(
                            rows_sb[:, t % 2, i, :], None, tables[f],
                            bass.IndirectOffsetOnAxis(ap=ids_sb[:, t, f:f + 1], axis=0),
                        ).then_inc(gathered[t][k], 16)

        def copy_on(engine):
            return nc.vector.tensor_copy if engine == 0 else nc.scalar.copy

        def empty_fill(eng, engine, n):
            bank = fill_ps[n % FILL_BANKS]
            eng.wait_ge(filled, n + 1)
            item = FILLS[n]
            if item[0] == "bottom":
                src = bank[:].rearrange("d (t p) -> d p t", t=TILES)
                dst = feat[:, :, 0].rearrange("d (p t) -> d p t", t=TILES)
                nc.scalar.copy(bottom_hi[:], bank[:]).then_inc(bottom_hi_ready, 1)
            elif item[0] == "one_hot":
                src, dst = bank[:], feat[:, :, 1 + item[1]]
                if item[1] == LATE:
                    src = bank[:, 0:LATE_SAMPLES].rearrange("d (b t) -> d b t", t=TILES - LATE_FROM)
                    dst = late(feat[:, :, FEATURES - 1])
            elif item[0] == "turn":
                empty_turn(engine, item, bank)
                return
            else:
                _, t, k = item
                count, first = len(group(t, k)), FIRST_GATHERED + GROUPS[k][0]
                src = bank[:, 0:count * P].rearrange("d (i p) -> d p i", i=count)
                dst = feat[:, t::TILES, first:first + count]
            copy_on(engine)(dst, src).then_inc(emptied[engine], 1)

        def empty_turn(engine, item, bank):
            blocks, t = turned_by(item), item[1]
            src = bank[:, 0:len(blocks) * P].rearrange("n (b s) -> n b s", s=P)
            hi = turned_hi[:, t % 2, blocks.start:blocks.stop]
            if engine == 1:
                nc.scalar.copy(hi, src).then_inc(turned_hi_ready, 1)
            else:
                nc.vector.wait_ge(turned_hi_ready, TURNS.index(item) + 1)
                nc.vector.tensor_tensor(turned_lo[:, t % 2, blocks.start:blocks.stop], src, hi.bitcast(F32),
                                        ALU.subtract).then_inc(emptied[0], 1)

        def empty_gram(eng, engine, t, r):
            eng.wait_ge(gram_done, ROUNDS * t + r + 1)
            if t >= 1:
                eng.wait_ge(z_hi_ready, ROUNDS * (t - 1) + r + 1)
                eng.wait_ge(z_lo_ready, ROUNDS * (t - 1) + r + 1)
            samples = slice(r * CLASS // ROUNDS, (r + 1) * CLASS // ROUNDS)
            for j in range(CLASSES):
                if j // 2 != engine:
                    continue
                for c in range(CLASSES):
                    chunks = len(range(c, FEATURES, CLASSES))
                    src = gram_ps[CLASS * j:CLASS * j + FEATURES, samples, c:FEATURES:CLASSES]
                    dst = z[CLASS * c:CLASS * c + FEATURES, 0:chunks, j, r]
                    last = copy_on(engine)(dst, src.rearrange("f s g -> f g s"))
            last.then_inc(z_ready[engine], 1)

        def layer1_parts(t):
            half = HIDDEN1 // 2
            if t < LAST:
                return [(h1_ps, slice(0, HIDDEN1))]
            return [(h1_ps, slice(0, half)), (h1_ps_last, slice(half, HIDDEN1))]

        def turned_by(item):
            blocks = range(HIDDEN1 // P)
            return blocks if len(item) == 2 else blocks[item[2] * len(blocks) // 2:(item[2] + 1) * len(blocks) // 2]

        def round_of(tensor, r):
            return tensor.rearrange("k c (j r s) -> k c j r s", j=CLASSES, r=ROUNDS)[:, :, :, r]

        @block.vector
        def _(dve):
            nc.vector.memset(z[:], 1.0).then_inc(z_preset, 1)
            dve.wait_ge(iota_ready, 1)
            nc.vector.tensor_copy(row_number[:], row_number_i[:]).then_inc(row_number_ready, 1)
            dve.wait_ge(row_number_ready, 1)

            def make_one_hot(n):
                if n >= 2:
                    dve.wait_ge(filled, looked_up(n - 2))
                dve.wait_ge(ids_spread[n], 16)
                for at, c in enumerate(BY_VECTOR):
                    if at == LOW_PART_AT and n >= 2:
                        make_low_part(n)
                    nc.vector.tensor_scalar(like_ids(one_hot_chunk(n, c), n), ids_looked_up(n),
                                            row_number[0:SPREAD, c:c + 1], None,
                                            ALU.is_equal).then_inc(one_hot_by_vector_ready, 1)
                if n < 2:
                    make_low_part(n)

            def make_low_part(n):
                dve.wait_ge(table_hi_ready, n + 1)
                nc.vector.tensor_tensor(table_lo[0:SPREAD, n % 2], raw("table", n)[0:SPREAD],
                                        table_hi[0:SPREAD, n % 2].bitcast(F32),
                                        ALU.subtract).then_inc(table_lo_ready, 1)

            def split_w1(i):
                dve.wait_ge(w1_hi_ready, i + 1)
                nc.vector.tensor_tensor(w1_lo[:, i * W1_PIECE:(i + 1) * W1_PIECE], raw("w1", i),
                                        w1_hi[:, i * W1_PIECE:(i + 1) * W1_PIECE].bitcast(F32),
                                        ALU.subtract).then_inc(w1_lo_ready, 1)

            make_one_hot(0)
            make_one_hot(1)
            for item in WORK:
                if item in FILLS:
                    n = FILLS.index(item)
                    if emptied_by(n) == 0:
                        empty_fill(dve, 0, n)
                    if item[0] == "one_hot" and item[1] + 2 < len(ONE_HOT):
                        make_one_hot(item[1] + 2)
                    if item == ("one_hot", len(ONE_HOT) - 3):
                        dve.wait_ge(bottom_hi_ready, 1)
                        dve.wait_ge(emptied[1], fills_of(1, FILLS.index(("bottom",)) + 1))
                        nc.vector.tensor_tensor(bottom_lo[:].rearrange("d (t p) -> d t p", t=TILES),
                                                feat[:, :, 0].rearrange("d (p t) -> d t p", t=TILES),
                                                bottom_hi[:].bitcast(F32).rearrange("d (t p) -> d t p", t=TILES),
                                                ALU.subtract).then_inc(bottom_lo_ready, 1)
                    for i in range(W1_PIECES):
                        if W1_AFTER[i] == n:
                            split_w1(i)
                elif item[0] == "gram":
                    t = item[1]
                    if t == 0:
                        dve.wait_ge(z_preset, 1)
                    for r in range(ROUNDS):
                        empty_gram(dve, 0, t, r)
                    for r in range(ROUNDS):
                        dve.wait_ge(z_hi_ready, ROUNDS * t + r + 1)
                        nc.vector.tensor_tensor(round_of(z_lo[:, t % 2], r), z[:, :, :, r],
                                                round_of(z_hi[:, t % 2].bitcast(F32), r),
                                                ALU.subtract).then_inc(z_lo_ready, 1)
                    if t == 0:
                        make_one_hot(LATE)
                elif item[0] == "layer1":
                    t = item[1]
                    for part, (bank, columns) in enumerate(layer1_parts(t)):
                        dve.wait_ge(layer1_done, t + part + 1)
                        nc.vector.tensor_scalar_max(h1[0:HALF, t % 2, columns], bank[0:HALF, columns],
                                                    0.0).then_inc(h1_ready[0], 1)
                    if t == 0:
                        dve.wait_ge(w2_hi_ready, 1)
                        dve.wait_ge(b2_hi_ready, 1)
                        nc.vector.tensor_tensor(w2_lo, w2_sb[:], w2_hi.bitcast(F32),
                                                ALU.subtract).then_inc(w2_lo_ready, 1)
                        nc.vector.tensor_tensor(b2_lo, b2_row, b2_hi.bitcast(F32),
                                                ALU.subtract).then_inc(b2_lo_ready, 1)
                        nc.vector.tensor_scalar(ones, identity[0:1], 0.0, 1.0,
                                                ALU.mult, ALU.add).then_inc(ones_ready, 1)
                elif item[0] == "layer2":
                    t = item[1]
                    dve.wait_ge(layer2_done, t + 1)
                    if t:
                        dve.wait_ge(y_ready, t)
                    nc.vector.scalar_tensor_tensor(h2, h2_ps, 0.0, w3_spread, ALU.max, ALU.mult,
                                                   accum_out=y_sb[:, t:t + 1]).then_inc(y_ready, 1)

        @block.scalar
        def _(act):
            def split_table(n):
                act.wait_ge(table_loaded[n], 32)
                if n >= 2:
                    act.wait_ge(filled, looked_up(n - 2))
                nc.scalar.copy(table_hi[0:SPREAD, n % 2], raw("table", n)[0:SPREAD]).then_inc(table_hi_ready, 1)
                act.wait_ge(ids_spread[n], 16)
                for at, c in enumerate(BY_SCALAR):
                    done = n * len(BY_SCALAR) + at
                    if done:
                        act.wait_ge(one_hot_by_scalar_ready, done)
                    away = distance[0:SPREAD, 0:samples_looked_up(n)]
                    nc.scalar.activation(like_ids(away, n), ids_looked_up(n), ACT.Abs,
                                         bias=minus_row[0:SPREAD, c:c + 1]).then_inc(distance_ready, 1)
                    act.wait_ge(distance_ready, done + 1)
                    nc.scalar.activation(one_hot_chunk(n, c), away, ACT.Relu, bias=one[0:SPREAD],
                                         scale=-1.0).then_inc(one_hot_by_scalar_ready, 1)

            def split_w1(i):
                act.wait_ge(w1_loaded[i], 16)
                nc.scalar.copy(w1_hi[:, i * W1_PIECE:(i + 1) * W1_PIECE], raw("w1", i)).then_inc(w1_hi_ready, 1)

            act.wait_ge(row_number_ready, 1)
            nc.scalar.mul(minus_row[:], row_number[:], -1.0).then_inc(minus_row_ready, 1)
            act.wait_ge(minus_row_ready, 1)
            act.wait_ge(one_ready, 1)
            split_table(0)
            split_table(1)
            for item in WORK:
                if item in FILLS:
                    n = FILLS.index(item)
                    if emptied_by(n) == 1 or item[0] == "turn":
                        empty_fill(act, 1, n)
                    if item[0] == "one_hot" and item[1] + 2 < len(ONE_HOT):
                        split_table(item[1] + 2)
                    for i in range(W1_PIECES):
                        if W1_AFTER[i] == n:
                            split_w1(i)
                elif item[0] == "gram":
                    t = item[1]
                    if t == 0:
                        act.wait_ge(z_preset, 1)
                    for r in range(ROUNDS):
                        empty_gram(act, 1, t, r)
                        act.wait_ge(z_ready[0], ROUNDS * t + r + 1)
                        act.wait_ge(z_ready[1], ROUNDS * t + r + 1)
                        if t >= 2:
                            act.wait_ge(layer1_done, t - 1)
                        nc.scalar.copy(round_of(z_hi[:, t % 2], r), z[:, :, :, r]).then_inc(z_hi_ready, 1)
                    if t == 0:
                        split_table(LATE)
                elif item[0] == "layer1":
                    t = item[1]
                    for part, (bank, columns) in enumerate(layer1_parts(t)):
                        act.wait_ge(layer1_done, t + part + 1)
                        nc.scalar.activation(h1[HALF:P, t % 2, columns], bank[HALF:P, columns],
                                             ACT.Relu).then_inc(h1_ready[1], 1)
                    if t == 0:
                        act.wait_ge(filled, looked_up(LATE - 1))
                        act.wait_ge(weights_loaded, 16 * 3)
                        nc.scalar.copy(w2_hi, w2_sb[:]).then_inc(w2_hi_ready, 1)
                        nc.scalar.copy(b2_hi, b2_row).then_inc(b2_hi_ready, 1)

        @block.tensor
        def _(pe):
            def bank_free(n):
                m = n - FILL_BANKS
                if m >= 0:
                    pe.wait_ge(emptied[emptied_by(m)], fills_of(emptied_by(m), m + 1))

            def all_emptied(n):
                for engine in (0, 1):
                    pe.wait_ge(emptied[engine], fills_of(engine, n))

            def fill(n):
                item = FILLS[n]
                bank = fill_ps[n % FILL_BANKS]
                bank_free(n)
                if item[0] == "bottom":
                    pe.wait_ge(identity_ready, 1)
                    pe.wait_ge(bottom_loaded, 16)
                    for t in range(TILES):
                        last = nc.tensor.transpose(bank[:, t * P:(t + 1) * P], bottom_sb[:, t], identity[:])
                    last.then_inc(filled, 1)
                elif item[0] == "group":
                    _, t, k = item
                    pe.wait_ge(gathered[t][k], 16 * len(group(t, k)))
                    for at, i in enumerate(group(t, k)):
                        last = nc.tensor.transpose(bank[:, at * P:(at + 1) * P], rows_sb[:, t % 2, i], identity[:])
                    last.then_inc(filled, 1)
                elif item[0] == "turn":
                    for engine in (0, 1):
                        pe.wait_ge(h1_ready[engine], item[1] + 1 + sum(item[2:]))
                    for at, nb in enumerate(turned_by(item)):
                        last = nc.tensor.transpose(bank[:, at * P:(at + 1) * P], h1[:, item[1] % 2, nb * P:(nb + 1) * P],
                                                   identity[:])
                    last.then_inc(filled, 1)
                else:
                    m = item[1]
                    into = bank[:, 0:samples_looked_up(m)]
                    pe.wait_ge(table_hi_ready, m + 1)
                    for c in range(CHUNKS):
                        if c in BY_SCALAR:
                            pe.wait_ge(one_hot_by_scalar_ready, len(BY_SCALAR) * m + BY_SCALAR.index(c) + 1)
                        else:
                            pe.wait_ge(one_hot_by_vector_ready, len(BY_VECTOR) * m + BY_VECTOR.index(c) + 1)
                        nc.tensor.matmul(into, table_hi[0:SPREAD, m % 2, c], one_hot_chunk(m, c),
                                         start=(c == 0), stop=False)
                    pe.wait_ge(table_lo_ready, m + 1)
                    for c in range(CHUNKS):
                        last = nc.tensor.matmul(into, table_lo[0:SPREAD, m % 2, c], one_hot_chunk(m, c),
                                                start=False, stop=(c == CHUNKS - 1))
                    last.then_inc(filled, 1)

            def gram(t):
                all_emptied(needed_by(t))
                for r in range(ROUNDS):
                    if t >= 1:
                        for engine in (0, 1):
                            pe.wait_ge(z_ready[engine], ROUNDS * (t - 1) + r + 1)
                    for s in range(r * CLASS // ROUNDS, (r + 1) * CLASS // ROUNDS):
                        for j in range(CLASSES):
                            e = feat[:, TILES * (CLASS * j + s) + t, :]
                            last = nc.tensor.matmul(gram_ps[CLASS * j:CLASS * j + FEATURES, s, 0:FEATURES], e, e,
                                                    start=True, stop=True)
                    last.then_inc(gram_done, 1)

            def layer1(t):
                if t == 0:
                    pe.wait_ge(bottom_hi_ready, 1)
                    pe.wait_ge(bottom_lo_ready, 1)
                    pe.wait_ge(w1_lo_ready, W1_PIECES)
                tile = slice(t * P, (t + 1) * P)
                for part, (bank, columns) in enumerate(layer1_parts(t)):
                    for engine in (0, 1):
                        if part == 1:
                            pe.wait_ge(z_ready[engine], ROUNDS * (t + 1))
                        elif t >= 1:
                            pe.wait_ge(h1_ready[engine], t)
                    for x, w in ((bottom_hi, w1_hi), (bottom_hi, w1_lo), (bottom_lo, w1_hi)):
                        nc.tensor.matmul(bank[:, columns], x[:, tile], w[:, Z_CHUNKS, columns],
                                         start=(x is bottom_hi and w is w1_hi), stop=False)
                for bank, columns in layer1_parts(t):
                    into = bank[:, columns]
                    pe.wait_ge(z_hi_ready, ROUNDS * (t + 1))
                    for g in range(Z_CHUNKS):
                        nc.tensor.matmul(into, z_hi[:, t % 2, g], w1_hi[:, g, columns], start=False, stop=False)
                        nc.tensor.matmul(into, z_hi[:, t % 2, g], w1_lo[:, g, columns], start=False, stop=False)
                    pe.wait_ge(z_lo_ready, ROUNDS * (t + 1))
                    for g in range(Z_CHUNKS):
                        last = nc.tensor.matmul(into, z_lo[:, t % 2, g], w1_hi[:, g, columns], start=False,
                                                stop=(g == Z_CHUNKS - 1))
                    last.then_inc(layer1_done, 1)

            def bias(t):
                if t == 0:
                    for ready in (w2_hi_ready, w2_lo_ready, b2_hi_ready, b2_lo_ready, ones_ready):
                        pe.wait_ge(ready, 1)
                else:
                    pe.wait_ge(y_ready, t)
                nc.tensor.matmul(h2_ps, ones, b2_hi, start=True, stop=False)
                nc.tensor.matmul(h2_ps, ones, b2_lo, start=False, stop=False)

            def layer2(t):
                for turn in TURNS:
                    if turn[1] != t:
                        continue
                    blocks = turned_by(turn)
                    pe.wait_ge(turned_hi_ready, TURNS.index(turn) + 1)
                    for nb in blocks:
                        nc.tensor.matmul(h2_ps, turned_hi[:, t % 2, nb], w2_hi[:, nb], start=False, stop=False)
                        nc.tensor.matmul(h2_ps, turned_hi[:, t % 2, nb], w2_lo[:, nb], start=False, stop=False)
                    pe.wait_ge(emptied[0], fills_of(0, FILLS.index(turn) + 1))
                    for nb in blocks:
                        last = nc.tensor.matmul(h2_ps, turned_lo[:, t % 2, nb], w2_hi[:, nb], start=False,
                                                stop=(nb == HIDDEN1 // P - 1))
                last.then_inc(layer2_done, 1)

            def warm_up():
                pe.wait_ge(identity_ready, 1)
                for _ in range(WARM_UP):
                    nc.tensor.transpose(h1_ps[:, 0:P], identity[:], identity[:])

            warm_up()
            fills = 0
            for item in WORK:
                if item in FILLS:
                    fill(fills)
                    fills += 1
                elif item[0] == "gram":
                    gram(item[1])
                elif item[0] == "layer1":
                    layer1(item[1])
                elif item[0] == "bias":
                    bias(item[1])
                else:
                    layer2(item[1])


def kernel(**inputs):
    import numpy as np
    import concourse.bacc as bacc
    from concourse.bass_utils import run_bass_kernel_spmd

    nc = bacc.Bacc("TRN2", target_bir_lowering=False, num_devices=1)
    arrays = {}

    def give(name, a):
        a = np.ascontiguousarray(a)
        arrays[name] = a
        return nc.dram_tensor(name, a.shape, mybir.dt.from_np(a.dtype), kind="ExternalInput").ap()

    w1 = np.asarray(inputs["W_top1"])
    pair = np.zeros((FEATURES, FEATURES), np.int64)
    pair[np.triu_indices(FEATURES, k=1)] = np.arange(FEATURES * (FEATURES - 1) // 2)
    pairs = np.zeros((P, W1_CHUNKS, HIDDEN1), w1.dtype)
    for j in range(FEATURES):
        for i in range(j):
            lo, hi = sorted((POSITIONS[i], POSITIONS[j]))
            pairs[CLASS * (j % CLASSES) + i, j // CLASSES] = w1[pair[lo, hi]]
    pairs[FEATURES, 0] = np.asarray(inputs["b_top1"])
    pairs[:, Z_CHUNKS] = w1[w1.shape[0] - D:]

    ids = np.asarray(inputs["ids"])
    out = nc.dram_tensor("y", (BATCH, 1), F32, kind="ExternalOutput").ap()
    build(nc, give("bottom", inputs["r_bottom_output"]), give("ids", ids), give("ids_by_table", ids.T),
          [give(f"tbl_{f}", inputs[f"tbl_{f}"]) for f in range(TABLES)], give("w1", pairs),
          give("w2", inputs["W_top2"]), give("b2", inputs["b_top2"]), give("w3", inputs["W_top3"]), out)
    return run_bass_kernel_spmd(nc, [arrays], core_ids=[0]).results[0]["y"]
```
